# Optimizing a Trainium2 kernel written in Bass

```python
import numpy as np
import jax
import jax.numpy as jnp

def _softmax(x, axis=-1):
    return jax.nn.softmax(x, axis=axis)

def _gelu(x):
    return jax.nn.gelu(x, approximate=True)

def _silu(x):
    return jax.nn.silu(x)

def _sigmoid(x):
    return jax.nn.sigmoid(x)

def _layernorm(x, axis=-1, eps=1e-05):
    m = jnp.mean(x, axis=axis, keepdims=True)
    v = jnp.var(x, axis=axis, keepdims=True)
    return (x - m) / jnp.sqrt(v + eps)

def _scatter_add(tgt, idx, src, axis=0):
    return tgt.at[idx].add(src)

def _segment_sum(src, seg, n):
    return jax.ops.segment_sum(src, seg, n)
kernel_name = 'mk_vit_tower_d1_tok_img256_r4_2e78d6'

def setup_inputs(seed: int=0):
    np.random.seed(seed)
    _w = jnp.asarray

    def _rec_inputs():
        import jax
        import jax.numpy as jnp
        _rk = jax.random.key(seed)
        x = -0.000125008 + 0.999885 * jax.random.normal(jax.random.fold_in(_rk, 1), (4, 64, 64, 64), jnp.float32)
        return x
    x = _rec_inputs()

    def _L0_tok_setup():
        import jax, jax.numpy as jnp
        import numpy as np
        DIM = 64
        NH = 8
        WH, WW = (8, 8)

        def _rope_axis(x, axis):
            half = x.shape[-1]
            inv_freq = 1.0 / 10000.0 ** (jnp.arange(0, half, 2, dtype=jnp.float32) / half)
            pos = jnp.arange(x.shape[axis], dtype=jnp.float32)
            ang = pos[:, None] * inv_freq
            cos, sin = (jnp.cos(ang), jnp.sin(ang))
            shape = [1, 1, 1, ang.shape[-1]]
            shape[axis] = ang.shape[0]
            cos = cos.reshape(shape).astype(x.dtype)
            sin = sin.reshape(shape).astype(x.dtype)
            x1, x2 = (x[..., 0::2], x[..., 1::2])
            r1 = x1 * cos - x2 * sin
            r2 = x1 * sin + x2 * cos
            return jnp.stack([r1, r2], axis=-1).reshape(x.shape)

        def _rope2(x):
            half = x.shape[-1] // 2
            return jnp.concatenate([_rope_axis(x[..., :half], 1), _rope_axis(x[..., half:], 2)], axis=-1)
        key = jax.random.key(seed)
        ks = jax.random.split(key, 5)
        B, H, W, C = (32, 64, 64, DIM)
        s = 1.0 / np.sqrt(C)
        return {'x': jax.random.normal(ks[0], (B, H, W, C), dtype=jnp.float32), 'qkv_w': jax.random.uniform(ks[1], (3 * C, C), jnp.float32, -s, s), 'qkv_b': jax.random.uniform(ks[2], (3 * C,), jnp.float32, -s, s), 'proj_w': jax.random.uniform(ks[3], (C, C), jnp.float32, -s, s), 'proj_b': jax.random.uniform(ks[4], (C,), jnp.float32, -s, s)}
    _L0_tok_all = _L0_tok_setup()
    _L0_tok_in = {k: v for k, v in _L0_tok_all.items() if k in ('qkv_w', 'qkv_b', 'proj_w', 'proj_b')}
    del _L0_tok_all

    def _L0_attn_setup():
        import jax, jax.numpy as jnp
        import numpy as np
        D_MODEL, D_STATE, D_CONV, EXPAND = (64, 16, 4, 2)
        D_INNER = D_MODEL * EXPAND
        RMS_EPS = 1.1920929e-07

        def _mamba_fwd(x, norm_w, in_proj_w, conv_w, conv_b, A_log, projB_w, projC_w, projDelta_w, projDelta_b, D, out_proj_w):
            B, L, _ = x.shape
            residual = x
            xn = x * jax.lax.rsqrt(jnp.mean(x * x, axis=-1, keepdims=True) + RMS_EPS) * norm_w
            xz = xn @ in_proj_w.T
            x_branch, z = jnp.split(xz, 2, axis=-1)
            xc = jnp.transpose(x_branch, (0, 2, 1))
            xc = jax.lax.conv_general_dilated(xc, conv_w, window_strides=(1,), padding=[(D_CONV - 1, 0)], dimension_numbers=('NCH', 'OIH', 'NCH'), feature_group_count=D_INNER)
            xc = xc + conv_b[None, :, None]
            x_branch = jax.nn.silu(jnp.transpose(xc, (0, 2, 1)))
            delta = jax.nn.softplus(x_branch @ projDelta_w.T + projDelta_b)
            B_t = x_branch @ projB_w.T
            C_t = x_branch @ projC_w.T
            A = -jnp.exp(A_log)
            dA = jnp.exp(delta[..., None] * A[None, None])
            x_db = (x_branch * delta)[..., None] * B_t[:, :, None, :]

            def step(h, inp):
                dA_t, xdb_t, c_t = inp
                h = dA_t * h + xdb_t
                y_t = jnp.einsum('bdn,bn->bd', h, c_t)
                return (h, y_t)
            h0 = jnp.zeros((B, D_INNER, D_STATE), x.dtype)
            _, y = jax.lax.scan(step, h0, (jnp.swapaxes(dA, 0, 1), jnp.swapaxes(x_db, 0, 1), jnp.swapaxes(C_t, 0, 1)))
            y = jnp.swapaxes(y, 0, 1)
            y = y + x_branch * D
            y = y * jax.nn.silu(z)
            return y @ out_proj_w.T + residual
        key = jax.random.key(seed)
        ks = jax.random.split(key, 12)
        s = lambda fan_in: 1.0 / np.sqrt(fan_in)
        return {'x': jax.random.normal(ks[0], (4, 512, D_MODEL), dtype=jnp.float32), 'norm_w': jnp.ones((D_MODEL,), jnp.float32), 'in_proj_w': jax.random.uniform(ks[1], (2 * D_INNER, D_MODEL), jnp.float32, -s(D_MODEL), s(D_MODEL)), 'conv_w': jax.random.uniform(ks[2], (D_INNER, 1, D_CONV), jnp.float32, -s(D_CONV), s(D_CONV)), 'conv_b': jax.random.uniform(ks[3], (D_INNER,), jnp.float32, -s(D_CONV), s(D_CONV)), 'A_log': jax.random.normal(ks[4], (D_INNER, D_STATE), jnp.float32), 'projB_w': jax.random.uniform(ks[5], (D_STATE, D_INNER), jnp.float32, -s(D_INNER), s(D_INNER)), 'projC_w': jax.random.uniform(ks[6], (D_STATE, D_INNER), jnp.float32, -s(D_INNER), s(D_INNER)), 'projDelta_w': jax.random.uniform(ks[7], (D_INNER, D_INNER), jnp.float32, -s(D_INNER), s(D_INNER)), 'projDelta_b': jax.random.uniform(ks[8], (D_INNER,), jnp.float32, -s(D_INNER), s(D_INNER)), 'D': jnp.ones((D_INNER,), jnp.float32), 'out_proj_w': jax.random.uniform(ks[9], (D_MODEL, D_INNER), jnp.float32, -s(D_INNER), s(D_INNER))}
    _L0_attn_all = _L0_attn_setup()
    _L0_attn_in = {k: v for k, v in _L0_attn_all.items() if k in ('norm_w', 'in_proj_w', 'conv_w', 'conv_b', 'A_log', 'projB_w', 'projC_w', 'projDelta_w', 'projDelta_b', 'D', 'out_proj_w')}
    del _L0_attn_all

    def _L0_ffn_setup():
        import jax, jax.numpy as jnp
        import numpy as np
        E, D, H, TOP_K = (6, 64, 64, 2)
        ROUTER_H = D // 2
        key = jax.random.key(seed)
        ks = jax.random.split(key, 12)
        s = 1.0 / np.sqrt(D)
        sh = 1.0 / np.sqrt(H)
        sr = 1.0 / np.sqrt(ROUTER_H)
        return {'features': jax.random.normal(ks[0], (8, 1024, D), dtype=jnp.float32), 'router_w1': jax.random.uniform(ks[1], (D, ROUTER_H), jnp.float32, -s, s), 'router_b1': jnp.zeros((ROUTER_H,), jnp.float32), 'router_w2': jax.random.uniform(ks[2], (ROUTER_H, E), jnp.float32, -sr, sr), 'router_b2': jnp.zeros((E,), jnp.float32), 'expert_w1': jax.random.uniform(ks[3], (E, D, H), jnp.float32, -s, s), 'expert_b1': jnp.zeros((E, H), jnp.float32), 'expert_w2': jax.random.uniform(ks[4], (E, H, H), jnp.float32, -sh, sh), 'expert_b2': jnp.zeros((E, H), jnp.float32), 'expert_w3': jax.random.uniform(ks[5], (E, H, D), jnp.float32, -sh, sh), 'expert_b3': jnp.zeros((E, D), jnp.float32)}
    _L0_ffn_all = _L0_ffn_setup()
    _L0_ffn_in = {k: v for k, v in _L0_ffn_all.items() if k in ('router_w1', 'router_b1', 'router_w2', 'router_b2', 'expert_w1', 'expert_b1', 'expert_w2', 'expert_b2', 'expert_w3', 'expert_b3')}
    del _L0_ffn_all
    return {'x': x, 'L0_tok_qkv_w': _L0_tok_in['qkv_w'], 'L0_tok_qkv_b': _L0_tok_in['qkv_b'], 'L0_tok_proj_w': _L0_tok_in['proj_w'], 'L0_tok_proj_b': _L0_tok_in['proj_b'], 'L0_attn_norm_w': _L0_attn_in['norm_w'], 'L0_attn_in_proj_w': _L0_attn_in['in_proj_w'], 'L0_attn_conv_w': _L0_attn_in['conv_w'], 'L0_attn_conv_b': _L0_attn_in['conv_b'], 'L0_attn_A_log': _L0_attn_in['A_log'], 'L0_attn_projB_w': _L0_attn_in['projB_w'], 'L0_attn_projC_w': _L0_attn_in['projC_w'], 'L0_attn_projDelta_w': _L0_attn_in['projDelta_w'], 'L0_attn_projDelta_b': _L0_attn_in['projDelta_b'], 'L0_attn_D': _L0_attn_in['D'], 'L0_attn_out_proj_w': _L0_attn_in['out_proj_w'], 'L0_ffn_router_w1': _L0_ffn_in['router_w1'], 'L0_ffn_router_b1': _L0_ffn_in['router_b1'], 'L0_ffn_router_w2': _L0_ffn_in['router_w2'], 'L0_ffn_router_b2': _L0_ffn_in['router_b2'], 'L0_ffn_expert_w1': _L0_ffn_in['expert_w1'], 'L0_ffn_expert_b1': _L0_ffn_in['expert_b1'], 'L0_ffn_expert_w2': _L0_ffn_in['expert_w2'], 'L0_ffn_expert_b2': _L0_ffn_in['expert_b2'], 'L0_ffn_expert_w3': _L0_ffn_in['expert_w3'], 'L0_ffn_expert_b3': _L0_ffn_in['expert_b3']}

def reference(x, L0_tok_qkv_w, L0_tok_qkv_b, L0_tok_proj_w, L0_tok_proj_b, L0_attn_norm_w, L0_attn_in_proj_w, L0_attn_conv_w, L0_attn_conv_b, L0_attn_A_log, L0_attn_projB_w, L0_attn_projC_w, L0_attn_projDelta_w, L0_attn_projDelta_b, L0_attn_D, L0_attn_out_proj_w, L0_ffn_router_w1, L0_ffn_router_b1, L0_ffn_router_w2, L0_ffn_router_b2, L0_ffn_expert_w1, L0_ffn_expert_b1, L0_ffn_expert_w2, L0_ffn_expert_b2, L0_ffn_expert_w3, L0_ffn_expert_b3):
    import jax
    import jax.numpy as jnp

    def _L0_tok_ref(x, qkv_w, qkv_b, proj_w, proj_b):
        import jax, jax.numpy as jnp
        import numpy as np
        DIM = 64
        NH = 8
        WH, WW = (8, 8)

        def _rope_axis(x, axis):
            half = x.shape[-1]
            inv_freq = 1.0 / 10000.0 ** (jnp.arange(0, half, 2, dtype=jnp.float32) / half)
            pos = jnp.arange(x.shape[axis], dtype=jnp.float32)
            ang = pos[:, None] * inv_freq
            cos, sin = (jnp.cos(ang), jnp.sin(ang))
            shape = [1, 1, 1, ang.shape[-1]]
            shape[axis] = ang.shape[0]
            cos = cos.reshape(shape).astype(x.dtype)
            sin = sin.reshape(shape).astype(x.dtype)
            x1, x2 = (x[..., 0::2], x[..., 1::2])
            r1 = x1 * cos - x2 * sin
            r2 = x1 * sin + x2 * cos
            return jnp.stack([r1, r2], axis=-1).reshape(x.shape)

        def _rope2(x):
            half = x.shape[-1] // 2
            return jnp.concatenate([_rope_axis(x[..., :half], 1), _rope_axis(x[..., half:], 2)], axis=-1)
        B, H, W, C = x.shape
        hd = C // NH
        N = WH * WW
        xw = x.reshape(B, H // WH, WH, W // WW, WW, C).transpose(0, 1, 3, 2, 4, 5).reshape(-1, N, C)
        qkv = xw @ qkv_w.T + qkv_b
        qkv = qkv.reshape(-1, N, 3, NH, hd).transpose(2, 0, 3, 1, 4)
        q, k, v = (qkv[0], qkv[1], qkv[2])
        q = _rope2(q.reshape(-1, WH, WW, hd)).reshape(-1, NH, N, hd)
        k = _rope2(k.reshape(-1, WH, WW, hd)).reshape(-1, NH, N, hd)
        scale = hd ** (-0.5)
        attn = jax.nn.softmax(q * scale @ jnp.swapaxes(k, -2, -1), axis=-1)
        out = (attn @ v).transpose(0, 2, 1, 3).reshape(-1, N, C)
        out = out.reshape(B, H // WH, W // WW, WH, WW, C).transpose(0, 1, 3, 2, 4, 5).reshape(B, H * W, C)
        return out @ proj_w.T + proj_b

    def _L0_attn_ref(x, norm_w, in_proj_w, conv_w, conv_b, A_log, projB_w, projC_w, projDelta_w, projDelta_b, D, out_proj_w):
        import jax, jax.numpy as jnp
        import numpy as np
        D_MODEL, D_STATE, D_CONV, EXPAND = (64, 16, 4, 2)
        D_INNER = D_MODEL * EXPAND
        RMS_EPS = 1.1920929e-07

        def _mamba_fwd(x, norm_w, in_proj_w, conv_w, conv_b, A_log, projB_w, projC_w, projDelta_w, projDelta_b, D, out_proj_w):
            B, L, _ = x.shape
            residual = x
            xn = x * jax.lax.rsqrt(jnp.mean(x * x, axis=-1, keepdims=True) + RMS_EPS) * norm_w
            xz = xn @ in_proj_w.T
            x_branch, z = jnp.split(xz, 2, axis=-1)
            xc = jnp.transpose(x_branch, (0, 2, 1))
            xc = jax.lax.conv_general_dilated(xc, conv_w, window_strides=(1,), padding=[(D_CONV - 1, 0)], dimension_numbers=('NCH', 'OIH', 'NCH'), feature_group_count=D_INNER)
            xc = xc + conv_b[None, :, None]
            x_branch = jax.nn.silu(jnp.transpose(xc, (0, 2, 1)))
            delta = jax.nn.softplus(x_branch @ projDelta_w.T + projDelta_b)
            B_t = x_branch @ projB_w.T
            C_t = x_branch @ projC_w.T
            A = -jnp.exp(A_log)
            dA = jnp.exp(delta[..., None] * A[None, None])
            x_db = (x_branch * delta)[..., None] * B_t[:, :, None, :]

            def step(h, inp):
                dA_t, xdb_t, c_t = inp
                h = dA_t * h + xdb_t
                y_t = jnp.einsum('bdn,bn->bd', h, c_t)
                return (h, y_t)
            h0 = jnp.zeros((B, D_INNER, D_STATE), x.dtype)
            _, y = jax.lax.scan(step, h0, (jnp.swapaxes(dA, 0, 1), jnp.swapaxes(x_db, 0, 1), jnp.swapaxes(C_t, 0, 1)))
            y = jnp.swapaxes(y, 0, 1)
            y = y + x_branch * D
            y = y * jax.nn.silu(z)
            return y @ out_proj_w.T + residual
        return _mamba_fwd(x, norm_w, in_proj_w, conv_w, conv_b, A_log, projB_w, projC_w, projDelta_w, projDelta_b, D, out_proj_w)

    def _L0_ffn_ref(features, router_w1, router_b1, router_w2, router_b2, expert_w1, expert_b1, expert_w2, expert_b2, expert_w3, expert_b3):
        import jax, jax.numpy as jnp
        import numpy as np
        E, D, H, TOP_K = (6, 64, 64, 2)
        ROUTER_H = D // 2
        rh = jax.nn.relu(features @ router_w1 + router_b1)
        expert_logits = jax.nn.softmax(rh @ router_w2 + router_b2, axis=-1)
        top_w, top_i = jax.lax.top_k(expert_logits, TOP_K)
        routing_weights = jax.nn.softmax(top_w, axis=-1)
        h1 = jax.nn.relu(jnp.einsum('bsd,edh->bseh', features, expert_w1) + expert_b1)
        h2 = jax.nn.relu(jnp.einsum('bseh,ehf->bsef', h1, expert_w2) + expert_b2)
        expert_out = jnp.einsum('bsef,efo->bseo', h2, expert_w3) + expert_b3
        sel = jnp.take_along_axis(expert_out, top_i[:, :, :, None], axis=2)
        combined = jnp.sum(sel * routing_weights[..., None], axis=2)
        return combined
    h = _L0_tok_ref(x, L0_tok_qkv_w, L0_tok_qkv_b, L0_tok_proj_w, L0_tok_proj_b)
    h = h + _L0_attn_ref(_layernorm(h, axis=-1), L0_attn_norm_w, L0_attn_in_proj_w, L0_attn_conv_w, L0_attn_conv_b, L0_attn_A_log, L0_attn_projB_w, L0_attn_projC_w, L0_attn_projDelta_w, L0_attn_projDelta_b, L0_attn_D, L0_attn_out_proj_w)
    h = h + _L0_ffn_ref(_layernorm(h, axis=-1), L0_ffn_router_w1, L0_ffn_router_b1, L0_ffn_router_w2, L0_ffn_router_b2, L0_ffn_expert_w1, L0_ffn_expert_b1, L0_ffn_expert_w2, L0_ffn_expert_b2, L0_ffn_expert_w3, L0_ffn_expert_b3)
    return h

_drawn_inputs = setup_inputs


def setup_inputs(seed=0):
    import zlib

    import numpy as np

    out = dict(_drawn_inputs(seed))
    spreads = {'L0_attn_norm_w': (1.0, 0.6),
     'L0_attn_D': (1.0, 0.6),
     'L0_ffn_router_b1': (0.0, 0.8),
     'L0_ffn_router_b2': (0.0, 0.8),
     'L0_ffn_expert_b1': (0.0, 2.0),
     'L0_ffn_expert_b2': (0.0, 2.0),
     'L0_ffn_expert_b3': (0.0, 0.8)}
    factors = {'L0_attn_A_log': 7.15,
     'L0_attn_projB_w': 5.283,
     'L0_attn_projC_w': 4.004,
     'L0_attn_projDelta_w': 8.0,
     'L0_attn_projDelta_b': 8.0,
     'L0_ffn_router_w1': 8.0,
     'L0_ffn_router_w2': 8.0,
     'L0_ffn_expert_w1': 8.0,
     'L0_ffn_expert_w2': 8.0,
     'L0_ffn_expert_w3': 8.0}
    for name, (base, spread) in spreads.items():
        noise = np.random.default_rng([zlib.crc32(name.encode()), seed]).standard_normal(out[name].shape)
        drawn = base * np.exp(spread * noise) if base else spread * noise
        out[name] = jnp.asarray(drawn.astype(out[name].dtype))
    for name, factor in factors.items():
        out[name] = (out[name] * factor).astype(out[name].dtype)
    return out
```

```python
from contextlib import ExitStack

import numpy as np

import concourse.bass as bass
from concourse import mybir

F32 = mybir.dt.float32
F32R = mybir.dt.float32r
ALU = mybir.AluOpType
ACT = mybir.ActivationFunctionType
X_AXIS = mybir.AxisListType.X

B, IMG, C = 4, 64, 64
HEADS, HD, WIN = 8, 8, 8
L = IMG * IMG
CH = 1024
NCH = B * L // CH
PER_IMAGE = L // CH
BAND = 512
NW = IMG // WIN
DI, NS, TAPS = 128, 16, 4
GD = 128 // NS
NU = DI // GD
E, EP, RH = 6, 3, 32
LN_EPS = 1e-5
RMS_EPS = 1.1920929e-07
SCALE = HD ** -0.5

PACKED = [("ident", 128), ("wq", 128), ("wq2", 128), ("wk", 128), ("wk2", 128), ("wv", 128), ("bias_qk", 4),
          ("cos", 64), ("sin", 64), ("headmask", 8), ("wp", 128), ("bv_rep", 128), ("wp_row", 64),
          ("normw", 1), ("conv_in", 128), ("conv_tap", 256), ("z_in", 128), ("conv_b", 1), ("delta_b", 1),
          ("d_skip", 1), ("wdelta", 128), ("wb", 128), ("wc", 128), ("a_log", NU), ("y_sel", 128),
          ("w_out", 64), ("rw1", 2 * RH), ("rb1", 1), ("rw2", E), ("rb2", E), ("rev", E),
          ("ew1", 2 * EP * 128), ("eb1", EP), ("ew2", EP * 128), ("eb2", EP), ("ew3", EP * C),
          ("eb3", NW * C), ("keep", NCH)]
SELECT = [("unit_sel", 8 * 128), ("w_sel", EP * 128)]


def columns(plan):
    at, out = 0, {}
    for name, n in plan:
        out[name] = (at, at + n)
        at += n
    return out, at


COL, N_PACKED = columns(PACKED)
SEL, N_SELECT = columns(SELECT)

A_BANKS = 3
A_USES = [("xT", 0), ("q", 1), ("q2", 2), ("k", 0), ("k2", 1), ("v0", 2), ("v1", 0)]
A_USES += [("S0", 1), ("S1", 2)]
for _w in range(NW):
    A_USES += [(f"T{_w}", 0)] + ([(f"S{_w + 2}", 1 + _w % 2)] if _w + 2 < NW else [])
A_USES += [("oT", 0), ("proj", 1), ("n0", 2), ("n1", 0), ("conv0", 1), ("conv1", 2), ("z0", 0), ("z1", 1),
           ("d0", 2), ("d1", 0), ("b0", 1), ("b1", 2), ("c0", 0), ("c1", 1)]
F_BANKS = 2
F_NAMES = ["mo", "fT", "r0", "r1", "lg", "wT0", "wT1", "wTT"]
for _s in range(2):
    for _e in range(EP):
        F_NAMES += [f"h1_{_s}{_e}", f"h2_{_s}{_e}", f"wb_{_s}{_e}"]
F_NAMES += ["out"]
if len(F_NAMES) % 2:
    F_NAMES.insert(0, "spare")
F_USES = [(n, i % 2) for i, n in enumerate(F_NAMES)]


F_AT = {"mean": 0, "square": 1, "variance": 2, "root": 3, "turn": 5, "router": 6, "route": 8, "weights": 11,
        "out": 29}
F_EXPERT = {13 + 2 * i: (i // EP, i % EP) for i in range(2 * EP)}


class Signal:

    def __init__(self, sem, per):
        self.sem, self.per = sem, per

    def at(self, chunk, k):
        value = chunk * self.per + k
        return max(value, 0) if isinstance(value, int) else value


class Use:

    def __init__(self, bank, filled, drained, index):
        self.bank, self.index = bank, index
        self.fills, self.drains = filled, drained
        self.filled, self.drained = filled.sem, drained.sem

    def opens(self, chunk):
        return self.drains.at(chunk, self.index)

    def full(self, chunk):
        return self.fills.at(chunk, self.index + 1)

    def empty(self, chunk):
        return self.drains.at(chunk, self.index + 1)


def tower(nc, x, packed, select, out):
    with ExitStack() as ctx:
        def sb(name, shape, dt=F32):
            return ctx.enter_context(nc.sbuf_tensor(name, shape, dt))

        def sem(name):
            return ctx.enter_context(nc.semaphore(name))

        def sig(name, per):
            return Signal(sem(name), per)

        psum = [ctx.enter_context(nc.psum_tensor(f"bank{i}", [128, 512], F32)) for i in range(8)]
        delta_ps, xd_ps, y_ps = [psum[0], psum[3]], [psum[1], psum[4]], psum[2]

        def bank_uses(stage, uses, first):
            count = [sum(b == bank for _, b in uses) for bank in range(max(b for _, b in uses) + 1)]
            signals = [(Signal(sem(f"{stage}_filled{b}"), n), Signal(sem(f"{stage}_drained{b}"), n))
                       for b, n in enumerate(count)]
            return {name: Use(psum[first + b], *signals[b], [n for n, x in uses if x == b].index(name))
                    for name, b in uses}

        A = bank_uses("a", A_USES, 3)
        F = bank_uses("f", F_USES, 6)

        wts = sb("wts", [128, N_PACKED])
        ident_r = sb("ident_r", [128, 128], F32R)
        unit_sel = sb("unit_sel", [128, 8, 128], F32R)
        w_sel = sb("w_sel", [2 * E, EP, 128], F32R)
        conv_w = sb("conv_w", [128, 2, 128])
        z_w = sb("z_w", [128, 128])
        a_neg = sb("a_neg", [128, NU])
        h_bias = sb("h_bias", [128, C])
        xin = sb("xin", [64, NW, 2, C])
        xT = sb("xT", [128, NW * 64])
        rot = sb("rot", [128, 4, 512])
        q_diag = sb("q_diag", [128, NW, 128])
        k_rot = sb("k_rot", [128, 512])
        k_heads = sb("k_heads", [128, NW, HEADS, 64])
        v_diag = sb("v_diag", [128, NW, 8, 18])
        neg_max = sb("neg_max", [128, 2, HEADS], F32R)
        probs = sb("probs", [128, 2, 512])
        probsT = sb("probsT", [128, 2, 512])
        rec = sb("rec", [128, 2, HEADS])
        attT = xT
        hid = sb("hid", [128, NW, C])
        att = hid
        cen = sb("cen", [128, NW, C])
        sq = sb("sq", [128, NW, C])
        lnx = cen
        xn = sq
        st_a = sb("st_a", [128, 20, NW])
        xnT = sb("xnT", [128, 3 + CH])
        relu_d, ex_d, ln_d, w_d = (rot[:, i, :] for i in range(4))
        delta = sb("delta", [128, CH])
        xdel = sb("xdel", [128, CH])
        xb = sb("xb", [128, CH])
        gate = sb("gate", [128, CH])
        delta_s = sb("delta_s", [128, 2, CH], F32R)
        xdel_s = sb("xdel_s", [128, 2, CH], F32R)
        b_rep = sb("b_rep", [128, CH])
        c_rep = sb("c_rep", [128, CH])
        h_ln = sb("h_ln", [128, NW, C])
        decay = sb("decay", [128, 2, BAND])
        inject = sb("inject", [128, 2, BAND])
        hs = sb("hs", [128, 4, BAND])
        hc = sb("hc", [128, 8, BAND])
        state = sb("state", [128, NU])
        y_skip = sb("y_skip", [128, BAND])
        y_gated = sb("y_gated", [128, NW, 2, 64])
        h1 = sb("h1", [128, NW, C])
        fcen = sb("fcen", [128, NW, C])
        fsq = sb("fsq", [128, NW, C])
        fn = fsq
        st_f = sb("st_f", [128, 20, NW])
        rt = sb("rt", [128, 14, NW, E])
        w_parts = sb("w_parts", [128, NW, 2, E], F32R)
        fT = sb("fT", [128, 512])
        rh = sb("rh", [RH, 2, 512])
        wT = sb("wT", [2 * E, 2, 512], F32R)
        wTT = sb("wTT", [NW * E, 128])
        e1 = sb("e1", [128, 2, 512])
        e2 = sb("e2", [128, 2, 512])
        ew = sb("ew", [128, 2, EP, 512])
        res = sb("res", [128, NW, C])
        staging = hc[:, 0:3, :].rearrange("p a b -> p (a b)")

        def col(name, a=0, b=None):
            lo, hi = COL[name]
            return wts[:, lo + a:(hi if b is None else lo + b)]

        def rows(name, n, a=0, b=None):
            lo, hi = COL[name]
            return wts[0:n, lo + a:(hi if b is None else lo + b)]

        loaded, staged = sem("loaded"), sem("staged")
        setup_pe, setup_act, setup_dve, setup_pool = sem("setup_pe"), sem("setup_act"), sem("setup_dve"), sem("setup_pool")
        x_in = sig("x_in", 16 * 16)
        roped = sig("roped", 4)
        q_ready = sig("q_ready", 2)
        k_ready = sig("k_ready", 1 + HEADS)
        max_ready = sig("max_ready", NW)
        scored = sig("scored", NW)
        shifted = sig("shifted", NW)
        probs_ready = sig("probs_ready", NW)
        rec_ready = sig("rec_ready", NW)
        ln1_dve = sig("ln1_dve", 16)
        ln1_act = sig("ln1_act", 5)
        ln1_pool = sig("ln1_pool", 4)
        tail_kept = sig("tail_kept", 1)
        soft_act = sig("soft_act", 4)
        soft_dve = sig("soft_dve", 4)
        soft_pool = sig("soft_pool", 4)
        xd_ready = sig("xd_ready", 1)
        split_a = sig("split_a", 4)
        split_b = sig("split_b", 4)
        delta_rep = sig("delta_rep", 2 * NU)
        xd_rep = sig("xd_rep", 2 * NU)
        decayed = sig("decayed", 2 * NU)
        injected = sig("injected", 2 * NU)
        scanned = sig("scanned", 2 * NU)
        weighted = sig("weighted", 2 * NU)
        stated = sig("stated", 2 * NU + 1)
        y_done = sig("y_done", 2)
        y_quads = sig("y_quads", 8)
        skipped = sig("skipped", 2)
        gated = sig("gated", 2)
        h1_ready = sig("h1_ready", 1)
        ln2_dve = sig("ln2_dve", 8)
        ln2_act = sig("ln2_act", 3)
        ln2_pool = sig("ln2_pool", 2)
        route_dve = sig("route_dve", 25)
        route_act = sig("route_act", 2)
        stored = sig("stored", 16 * 16)

        def unit(u):
            return 4 * (u % 4) + u // 4, u % 4, u // 4

        block = ctx.enter_context(nc.Block())

        @block.sync
        def _(sp):
            def load(c):
                if not isinstance(c, int) or c > 0:
                    sp.wait_ge(A["xT"].filled, A["xT"].full(c - 1))
                for par in range(2):
                    src = x[bass.ts(c * 2 + par, WIN), :, :].rearrange("i (w j) h -> i j w h", w=NW)
                    for r in range(WIN):
                        sp.dma_start(xin[8 * r:8 * r + 8, :, par, :], src[r]).then_inc(x_in.sem, 16)

            def store(c):
                sp.wait_ge(F["out"].drained, F["out"].empty(c))
                for par in range(2):
                    dst = out[bass.ts(c * 2 + par, WIN), :, :].rearrange("i (w j) h -> i j w h", w=NW)
                    for r in range(WIN):
                        at = 64 * par + 8 * r
                        sp.dma_start(dst[r], res[at:at + 8, :, :]).then_inc(stored.sem, 16)

            sp.dma_start(wts[:, :], packed).then_inc(loaded, 16)
            sp.dma_start(staging[:, 0:N_SELECT], select).then_inc(staged, 16)
            load(0)
            load(1)
            store(0)
            with sp.Fori(1, NCH - 1) as c:
                load(c + 1)
                store(c)
            store(NCH - 1)
            sp.wait_ge(stored.sem, stored.at(NCH - 1, 256))

        @block.tensor
        def _(pe):
            ident = col("ident")

            def turn(to, src, unit, waits):
                if waits:
                    return pe.matmul(to, src, unit, start=True, stop=True)
                return pe.transpose(to, src, unit)

            def a_front(c):
                use = A["xT"]
                pe.wait_ge(use.drained, use.opens(c))
                pe.wait_ge(x_in.sem, x_in.at(c, 256))
                for w in range(NW):
                    last = turn(use.bank[:, 64 * w:64 * w + 64], xin[:, w, :, :], wts[0:64, 0:64], w == 0)
                last.then_inc(use.filled, 1)
                pe.wait_ge(A["xT"].drained, A["xT"].empty(c))
                for name, wt in (("q", "wq"), ("q2", "wq2"), ("k", "wk"), ("k2", "wk2")):
                    use = A[name]
                    pe.wait_ge(use.drained, use.opens(c))
                    pe.matmul(use.bank[:, :], col(wt), xT[:, :], start=True, stop=True).then_inc(use.filled, 1)
                for v in range(2):
                    use = A[f"v{v}"]
                    pe.wait_ge(use.drained, use.opens(c))
                    for i in range(4):
                        w = 4 * v + i
                        for half in range(2):
                            last = pe.matmul(use.bank[64 * half:64 * half + 64, 128 * i:128 * i + 128],
                                             xT[:, 64 * w:64 * w + 64], col("wv"), start=True, stop=True)
                    last.then_inc(use.filled, 1)

            def a_scores(c, w):
                use = A[f"S{w}"]
                pe.wait_ge(use.drained, use.opens(c))
                if w == 0:
                    pe.wait_ge(q_ready.sem, q_ready.at(c, 2))
                    pe.wait_ge(k_ready.sem, k_ready.at(c, 1 + HEADS))
                pe.matmul(use.bank[:, :], q_diag[:, w, :], k_heads[:, w, :, :], start=True, stop=True)\
                  .then_inc(scored.sem, 1)

            def a_shift(c, w):
                pe.wait_ge(max_ready.sem, max_ready.at(c, w + 1))
                pe.matmul(A[f"S{w}"].bank[:, :], ident_r[:, :],
                          neg_max[:, w % 2, :].unsqueeze(2).to_broadcast([128, HEADS, 64]),
                          start=False, stop=True, skip_group_check=True).then_inc(shifted.sem, 1)

            def a_turn(c, w):
                use = A[f"T{w}"]
                pe.wait_ge(use.drained, use.opens(c))
                pe.wait_ge(probs_ready.sem, probs_ready.at(c, w + 1))
                for hp in range(4):
                    last = pe.transpose(use.bank[:, 128 * hp:128 * hp + 128], probs[:, w % 2, 128 * hp:128 * hp + 128],
                                        ident)
                last.then_inc(use.filled, 1)

            def a_pv(c, w):
                pe.wait_ge(A[f"T{w}"].drained, A[f"T{w}"].empty(c))
                if w == 0:
                    pe.wait_ge(A["v1"].drained, A["v1"].empty(c))
                    pe.wait_ge(A["v0"].drained, A["v0"].empty(c))
                use = A[f"S{w}"]
                for hp in range(4):
                    for par in range(2):
                        last = pe.matmul(use.bank[64 * par:64 * par + 64, 18 * hp:18 * hp + 18],
                                         probsT[:, w % 2, 128 * hp + 64 * par:128 * hp + 64 * par + 64],
                                         v_diag[:, w, 4 * par + hp, :], start=True, stop=True)
                last.then_inc(use.filled, 1)

            def a_attention(c):
                a_scores(c, 0)
                a_shift(c, 0)
                a_scores(c, 1)
                for w in range(NW):
                    if w + 1 < NW:
                        a_shift(c, w + 1)
                    a_turn(c, w)
                    a_pv(c, w)
                    if w + 2 < NW:
                        a_scores(c, w + 2)

            def a_project(c):
                use = A["oT"]
                pe.wait_ge(use.drained, use.opens(c))
                for i in range(4):
                    pe.wait_ge(A[f"S{2 * i}"].drained, A[f"S{2 * i}"].empty(c))
                    pe.wait_ge(A[f"S{2 * i + 1}"].drained, A[f"S{2 * i + 1}"].empty(c))
                    last = pe.transpose(use.bank[:, 128 * i:128 * i + 128], att[:, 2 * i:2 * i + 2, :], ident)
                last.then_inc(use.filled, 1)
                use = A["proj"]
                pe.wait_ge(use.drained, use.opens(c))
                pe.wait_ge(A["oT"].drained, A["oT"].empty(c))
                for i in range(4):
                    last = pe.matmul(use.bank[:, 128 * i:128 * i + 128], attT[:, 128 * i:128 * i + 128], col("wp"),
                                     start=True, stop=True)
                last.then_inc(use.filled, 1)

            def a_mamba_in(c):
                for n in range(2):
                    use = A[f"n{n}"]
                    pe.wait_ge(use.drained, use.opens(c))
                    pe.wait_ge(ln1_pool.sem, ln1_pool.at(c, 3))
                    for i in range(4):
                        last = turn(use.bank[0:64, 128 * i:128 * i + 128], xn[:, 4 * n + i, :], ident, i == 0)
                    last.then_inc(use.filled, 1)
                pe.wait_ge(A["n0"].drained, A["n0"].empty(c))
                pe.wait_ge(A["n1"].drained, A["n1"].empty(c))
                pe.wait_ge(tail_kept.sem, tail_kept.at(c, 1))
                for h in range(2):
                    use = A[f"conv{h}"]
                    pe.wait_ge(use.drained, use.opens(c))
                    pe.matmul(use.bank[:, :], conv_w[:, 0, :], xnT[:, 2 + BAND * h:2 + BAND * h + BAND],
                              start=True, stop=False)
                    pe.matmul(use.bank[:, :], conv_w[:, 1, :], xnT[:, BAND * h:BAND * h + BAND],
                              start=False, stop=True).then_inc(use.filled, 1)
                for h in range(2):
                    use = A[f"z{h}"]
                    pe.wait_ge(use.drained, use.opens(c))
                    pe.matmul(use.bank[:, :], z_w[:, :], xnT[:, 2 + BAND * h:2 + BAND * h + BAND],
                              start=True, stop=True).then_inc(use.filled, 1)
                for name, wt, src in (("d", "wdelta", "conv"), ("b", "wb", "conv"), ("c", "wc", "conv")):
                    for h in range(2):
                        use = A[f"{name}{h}"]
                        pe.wait_ge(use.drained, use.opens(c))
                        pe.wait_ge(A[f"conv{h}"].drained, A[f"conv{h}"].empty(c))
                        pe.matmul(use.bank[:, :], col(wt), xb[:, BAND * h:BAND * h + BAND],
                                  start=True, stop=True).then_inc(use.filled, 1)

            def m_spread(c, n):
                h, (g, _, _) = n // NU, unit(n % NU)
                if n == 0:
                    pe.wait_ge(split_b.sem, split_b.at(c, 4))
                if n == 1:
                    pe.wait_ge(A["c0"].drained, A["c0"].empty(c))
                    pe.wait_ge(A["c1"].drained, A["c1"].empty(c))
                if n >= 2:
                    pe.wait_ge(decayed.sem, decayed.at(c, n - 1))
                pe.matmul(delta_ps[n % 2][:, :], unit_sel[:, g % 8, :], delta_s[:, g // 8, BAND * h:BAND * h + BAND],
                          start=True, stop=True).then_inc(delta_rep.sem, 1)
                if n >= 2:
                    pe.wait_ge(injected.sem, injected.at(c, n - 1))
                pe.matmul(xd_ps[n % 2][:, :], unit_sel[:, g % 8, :], xdel_s[:, g // 8, BAND * h:BAND * h + BAND],
                          start=True, stop=True).then_inc(xd_rep.sem, 1)

            def m_collect(c, quad):
                h, i = quad // 4, quad % 4
                if i == 0:
                    pe.wait_ge(skipped.sem, skipped.at(c, h))
                for q in range(4):
                    n = 4 * quad + q
                    pe.wait_ge(weighted.sem, weighted.at(c, n + 1))
                    last = pe.matmul(y_ps[32 * q:32 * q + 32, :], col("y_sel", 32 * i, 32 * i + 32), hc[:, n % 8, :],
                                     start=(i == 0), stop=(i == 3))
                last.then_inc(y_quads.sem, 1)

            def m_scan(c, experts):
                for n in range(2 * NU):
                    m_spread(c, n)
                    if n % 4 == 2 and n >= 6:
                        m_collect(c, (n - 6) // 4)
                    if experts:
                        f_step(c - 1, n)
                m_collect(c, 7)

            def f_step(c, n):
                if n == F_AT["turn"]:
                    f_turn(c)
                if n == F_AT["router"]:
                    f_router(c)
                if n == F_AT["weights"]:
                    f_weights(c)
                if n in F_EXPERT:
                    f_expert(c, *F_EXPERT[n])
                if n == F_AT["out"]:
                    f_out(c)

            def f_front(c):
                if "spare" in F:
                    use = F["spare"]
                    pe.wait_ge(use.drained, use.opens(c))
                    pe.matmul(use.bank[:, 0:128], ident, ident, start=True, stop=True).then_inc(use.filled, 1)
                use = F["mo"]
                pe.wait_ge(use.drained, use.opens(c))
                pe.wait_ge(gated.sem, gated.at(c, 2))
                for w in range(NW):
                    last = pe.matmul(use.bank[:, C * w:C * w + C], y_gated[:, w, :, :], col("w_out"),
                                     start=True, stop=True)
                last.then_inc(use.filled, 1)

            def f_turn(c):
                use = F["fT"]
                pe.wait_ge(use.drained, use.opens(c))
                pe.wait_ge(ln2_pool.sem, ln2_pool.at(c, 2))
                for i in range(4):
                    last = pe.transpose(use.bank[:, 128 * i:128 * i + 128], fn[:, 2 * i:2 * i + 2, :], ident)
                last.then_inc(use.filled, 1)

            def f_router(c):
                pe.wait_ge(F["fT"].drained, F["fT"].empty(c))
                for s in range(2):
                    use = F[f"r{s}"]
                    pe.wait_ge(use.drained, use.opens(c))
                    pe.matmul(use.bank[0:RH, :], col("rw1", RH * s, RH * s + RH), fT[:, :], start=True, stop=True)\
                      .then_inc(use.filled, 1)
                use = F["lg"]
                pe.wait_ge(use.drained, use.opens(c))
                pe.wait_ge(F["r0"].drained, F["r0"].empty(c))
                pe.wait_ge(F["r1"].drained, F["r1"].empty(c))
                for w in range(NW):
                    at = 128 * (w // 2)
                    last = pe.matmul(use.bank[:, E * w:E * w + E], rh[:, w % 2, at:at + 128], rows("rw2", RH),
                                     start=True, stop=True)
                last.then_inc(use.filled, 1)

            def f_weights(c):
                pe.wait_ge(route_dve.sem, route_dve.at(c, 25))
                for s in range(2):
                    use = F[f"wT{s}"]
                    pe.wait_ge(use.drained, use.opens(c))
                    for i in range(4):
                        last = pe.transpose(use.bank[0:2 * E, 128 * i:128 * i + 128],
                                            w_parts[:, 2 * i + s, :, :].bitcast(F32), ident)
                    last.then_inc(use.filled, 1)
                use = F["wTT"]
                pe.wait_ge(use.drained, use.opens(c))
                turn(use.bank[0:NW * E, 0:128], rt[:, 13, :, :], ident, True).then_inc(use.filled, 1)

            def f_expert(c, s, e):
                use = F[f"h1_{s}{e}"]
                pe.wait_ge(use.drained, use.opens(c))
                at = 128 * (EP * s + e)
                pe.matmul(use.bank[:, :], col("ew1", at, at + 128), fT[:, :], start=True, stop=True)\
                  .then_inc(use.filled, 1)
                use = F[f"h2_{s}{e}"]
                pe.wait_ge(use.drained, use.opens(c))
                pe.wait_ge(F[f"h1_{s}{e}"].drained, F[f"h1_{s}{e}"].empty(c))
                pe.matmul(use.bank[:, :], col("ew2", 128 * e, 128 * e + 128), e1[:, e % 2, :],
                          start=True, stop=True).then_inc(use.filled, 1)
                use = F[f"wb_{s}{e}"]
                pe.wait_ge(use.drained, use.opens(c))
                pe.wait_ge(F[f"wT{s}"].drained, F[f"wT{s}"].empty(c))
                pe.matmul(use.bank[:, :], w_sel[:, e, :], wT[:, s, :], start=True, stop=True)\
                  .then_inc(use.filled, 1)

            def f_out(c):
                use = F["out"]
                pe.wait_ge(use.drained, use.opens(c))
                pe.wait_ge(F["wTT"].drained, F["wTT"].empty(c))
                pe.matmul(use.bank[:, :], wTT[:, :], rows("eb3", NW * E), start=True, stop=True)
                for s in range(2):
                    for e in range(EP):
                        pe.wait_ge(F[f"wb_{s}{e}"].drained, F[f"wb_{s}{e}"].empty(c))
                        for i in range(4):
                            w = 2 * i + s
                            last = pe.matmul(use.bank[:, C * w:C * w + C], ew[:, s, e, 128 * i:128 * i + 128],
                                             col("ew3", C * e, C * e + C), start=False,
                                             stop=True, skip_group_check=True)
                last.then_inc(use.filled, 1)

            def chunk(c, experts):
                a_front(c)
                a_attention(c)
                a_project(c)
                a_mamba_in(c)
                m_scan(c, experts)
                f_front(c)

            pe.wait_ge(loaded, 16)
            pe.matmul(y_ps[:, 0:C], rows("bv_rep", 65), rows("wp_row", 65), start=True, stop=True)\
              .then_inc(setup_pe, 1)
            pe.wait_ge(setup_dve, 9)
            pe.wait_ge(setup_pool, 4)
            pe.wait_ge(setup_act, 2)
            chunk(0, False)
            with pe.Fori(1, NCH) as c:
                chunk(c, True)
            for n in range(2 * NU):
                f_step(NCH - 1, n)

        @block.scalar
        def _(act):
            def tables(name):
                act.preload_act_table_set(name)

            def copy(out_, in_):
                return act.activation(out_, in_, ACT.Copy)

            def a_front(c):
                use = A["xT"]
                act.wait_ge(use.filled, use.full(c))
                copy(xT[:, :], use.bank[:, :]).then_inc(use.drained, 1)
                for v in range(2):
                    use = A[f"v{v}"]
                    act.wait_ge(use.filled, use.full(c))
                    for half in range(2):
                        p = slice(64 * half, 64 * half + 64)
                        last = copy(v_diag[p, 4 * v:4 * v + 4, :, 9 * half:9 * half + 8],
                                    use.bank[p, :].rearrange("p (w g c) -> p w g c", w=4, g=16)[:, :, 8 * half:8 * half + 8, :])
                    last.then_inc(use.drained, 1)

            def a_heads(c):
                act.wait_ge(k_ready.sem, k_ready.at(c, 1))
                for h in range(HEADS):
                    act.activation(k_heads[:, :, h, :], k_rot[:, :].rearrange("p (w j) -> p w j", w=NW), ACT.Copy,
                                   scale=col("headmask", h, h + 1)).then_inc(k_ready.sem, 1)

            def a_attention(c):
                for w in range(NW):
                    act.wait_ge(shifted.sem, shifted.at(c, w + 1))
                    act.activation(probs[:, w % 2, :], psum[4 + w % 2][:, :], ACT.Exp, scale=SCALE)\
                       .then_inc(probs_ready.sem, 1)
                    use = A[f"T{w}"]
                    act.wait_ge(use.filled, use.full(c))
                    copy(probsT[:, w % 2, :], use.bank[:, :]).then_inc(use.drained, 1)
                use = A["oT"]
                act.wait_ge(use.filled, use.full(c))
                copy(attT[:, :], use.bank[:, :]).then_inc(use.drained, 1)

            def inv_root(c, st, dve, k_in, mine, k_out):
                act.wait_ge(dve.sem, dve.at(c, k_in[0]))
                act.activation(st[:, k_out[1], :], st[:, k_in[1], :], ACT.Ln).then_inc(mine.sem, 1)
                act.wait_ge(mine.sem, mine.at(c, k_out[0]))
                act.activation(st[:, k_out[1] + 1, :], st[:, k_out[1], :], ACT.Exp, scale=-0.5).then_inc(mine.sem, 1)

            def a_norm(c):
                act.wait_ge(ln1_pool.sem, ln1_pool.at(c, 1))
                act.activation(sq[:, :, :], cen[:, :, :], ACT.Square).then_inc(ln1_act.sem, 1)
                inv_root(c, st_a, ln1_dve, (5, 3), ln1_act, (2, 4))
                inv_root(c, st_a, ln1_dve, (12, 11), ln1_act, (4, 12))

            def a_mamba_in(c):
                for n in range(2):
                    use = A[f"n{n}"]
                    act.wait_ge(use.filled, use.full(c))
                    if n == 0:
                        act.wait_ge(tail_kept.sem, tail_kept.at(c, 1))
                    for par in range(2):
                        for half in range(2):
                            at = 2 + half + BAND * par
                            dst = xnT[64 * half:64 * half + 64, at:at + BAND].rearrange(
                                "p (i w j) -> p w i j", i=8, w=8)[:, 4 * n:4 * n + 4, :, :]
                            src = use.bank[0:64, :].rearrange("p (w a i j) -> p w a i j", w=4, a=2, i=8)[:, :, par, :, :]
                            last = copy(dst, src)
                    last.then_inc(use.drained, 1)
                for h in range(2):
                    use = A[f"conv{h}"]
                    act.wait_ge(use.filled, use.full(c))
                    act.activation(xb[:, BAND * h:BAND * h + BAND], use.bank[:, :], ACT.Silu, bias=col("conv_b"))\
                       .then_inc(use.drained, 1)
                for h in range(2):
                    use = A[f"z{h}"]
                    act.wait_ge(use.filled, use.full(c))
                    act.activation(gate[:, BAND * h:BAND * h + BAND], use.bank[:, :], ACT.Silu).then_inc(use.drained, 1)
                tables("natural_log_exp_and_others")
                for h in range(2):
                    use = A[f"d{h}"]
                    act.wait_ge(use.filled, use.full(c))
                    act.wait_ge(soft_pool.sem, soft_pool.at(c, 2 * h))
                    act.activation(relu_d, use.bank[:, :], ACT.Relu, bias=col("delta_b"))
                    act.activation(w_d, use.bank[:, :], ACT.Abs, bias=col("delta_b")).then_inc(use.drained, 1)
                    act.wait_ge(A[f"d{h}"].drained, A[f"d{h}"].empty(c))
                    act.activation(ex_d, w_d, ACT.Exp, scale=-1.0).then_inc(soft_act.sem, 1)
                    act.wait_ge(soft_act.sem, soft_act.at(c, 2 * h + 1))
                    act.activation(ln_d, ex_d, ACT.Ln, bias=1.0).then_inc(soft_act.sem, 1)
                for name, dst in (("b", b_rep), ("c", c_rep)):
                    for h in range(2):
                        use = A[f"{name}{h}"]
                        act.wait_ge(use.filled, use.full(c))
                        copy(dst[:, BAND * h:BAND * h + BAND], use.bank[:, :]).then_inc(use.drained, 1)

            def m_decay(c, n):
                g, _, _ = unit(n % NU)
                act.wait_ge(delta_rep.sem, delta_rep.at(c, n + 1))
                act.wait_ge(scanned.sem, scanned.at(c, n - 1))
                act.activation(decay[:, n % 2, :], delta_ps[n % 2][:, :], ACT.Exp, scale=a_neg[:, g:g + 1])\
                   .then_inc(decayed.sem, 1)

            def f_front(c):
                if "spare" in F:
                    use = F["spare"]
                    act.wait_ge(use.filled, use.full(c))
                    copy(st_f[:, 19, 0:8], use.bank[:, 0:8]).then_inc(use.drained, 1)

            def f_square(c):
                act.wait_ge(ln2_pool.sem, ln2_pool.at(c, 1))
                act.activation(fsq[:, :, :], fcen[:, :, :], ACT.Square).then_inc(ln2_act.sem, 1)

            def f_turn(c):
                use = F["fT"]
                act.wait_ge(use.filled, use.full(c))
                copy(fT[:, :], use.bank[:, :]).then_inc(use.drained, 1)

            def f_router(c):
                for s in range(2):
                    use = F[f"r{s}"]
                    act.wait_ge(use.filled, use.full(c))
                    act.activation(rh[:, s, :], use.bank[0:RH, :], ACT.Relu, bias=rows("rb1", RH)).then_inc(use.drained, 1)

            def f_route(c):
                act.wait_ge(route_dve.sem, route_dve.at(c, 3))
                act.activation(rt[:, 2, :, :], rt[:, 1, :, :], ACT.Exp).then_inc(route_act.sem, 1)
                act.wait_ge(route_dve.sem, route_dve.at(c, 14))
                act.activation(st_f[:, 14, :], st_f[:, 13, :], ACT.Exp).then_inc(route_act.sem, 1)

            def f_weights(c):
                for s in range(2):
                    use = F[f"wT{s}"]
                    act.wait_ge(use.filled, use.full(c))
                    copy(wT[:, s, :], use.bank[0:2 * E, :]).then_inc(use.drained, 1)
                use = F["wTT"]
                act.wait_ge(use.filled, use.full(c))
                copy(wTT[:, :], use.bank[0:NW * E, 0:128]).then_inc(use.drained, 1)

            def f_expert(c, s, e):
                use = F[f"h1_{s}{e}"]
                act.wait_ge(use.filled, use.full(c))
                act.activation(e1[:, e % 2, :], use.bank[:, :], ACT.Relu, bias=col("eb1", e, e + 1))\
                   .then_inc(use.drained, 1)
                use = F[f"h2_{s}{e}"]
                act.wait_ge(use.filled, use.full(c))
                if s or e > 1:
                    act.wait_ge(F[f"wb_{(EP * s + e - 2) // EP}{(EP * s + e - 2) % EP}"].drained, F[f"wb_{(EP * s + e - 2) // EP}{(EP * s + e - 2) % EP}"].empty(c))
                act.activation(e2[:, (EP * s + e) % 2, :], use.bank[:, :], ACT.Relu, bias=col("eb2", e, e + 1))\
                   .then_inc(use.drained, 1)

            def f_step(c, n):
                if n == F_AT["square"]:
                    f_square(c)
                if n == F_AT["root"]:
                    inv_root(c, st_f, ln2_dve, (4, 3), ln2_act, (2, 4))
                if n == F_AT["turn"]:
                    f_turn(c)
                if n == F_AT["router"]:
                    f_router(c)
                if n == F_AT["route"]:
                    f_route(c)
                if n == F_AT["weights"]:
                    f_weights(c)
                if n in F_EXPERT:
                    f_expert(c, *F_EXPERT[n])

            def chunk(c, experts):
                a_front(c)
                a_heads(c)
                a_attention(c)
                a_norm(c)
                a_mamba_in(c)
                for n in range(2 * NU):
                    m_decay(c, n)
                    if experts:
                        f_step(c - 1, n)
                f_front(c)

            act.wait_ge(loaded, 16)
            act.activation(a_neg[:, :], col("a_log"), ACT.Exp).then_inc(setup_act, 1)
            act.wait_ge(setup_act, 1)
            act.activation(a_neg[:, :], a_neg[:, :], ACT.Copy, scale=-1.0).then_inc(setup_act, 1)
            act.wait_ge(setup_act, 2)
            tables("natural_log_exp_and_others")
            act.wait_ge(setup_pool, 4)
            act.wait_ge(setup_dve, 9)
            chunk(0, False)
            with act.Fori(1, NCH) as c:
                chunk(c, True)
            for n in range(2 * NU):
                f_step(NCH - 1, n)

        @block.vector
        def _(dve):
            def refine(c, st, done, k, v, r0, dst, tmp):
                dve.tensor_tensor(st[:, tmp, :], st[:, r0, :], st[:, r0, :], ALU.mult).then_inc(done.sem, 1)
                dve.wait_ge(done.sem, done.at(c, k + 1))
                dve.tensor_tensor(st[:, tmp + 1, :], st[:, tmp, :], st[:, v, :], ALU.mult).then_inc(done.sem, 1)
                dve.wait_ge(done.sem, done.at(c, k + 2))
                dve.tensor_scalar(st[:, tmp, :], st[:, tmp + 1, :], -0.5, 1.5, ALU.mult, ALU.add)\
                   .then_inc(done.sem, 1)
                dve.wait_ge(done.sem, done.at(c, k + 3))
                dve.tensor_tensor(st[:, dst, :], st[:, tmp, :], st[:, r0, :], ALU.mult).then_inc(done.sem, 1)

            def a_rope(c):
                for n, (name, tab) in enumerate((("q", "cos"), ("q2", "sin"), ("k", "cos"), ("k2", "sin"))):
                    use = A[name]
                    dve.wait_ge(use.filled, use.full(c))
                    if n == 0:
                        dve.wait_ge(k_ready.sem, k_ready.at(c - 1, 1))
                    dve.scalar_tensor_tensor(
                        out=rot[:, n, :].rearrange("p (w i) -> p w i", w=NW),
                        in0=use.bank[:, :].rearrange("p (w i) -> p w i", w=NW), scalar=col("bias_qk", n, n + 1),
                        in1=col(tab).unsqueeze(1).to_broadcast([128, NW, 64]),
                        op0=ALU.add, op1=ALU.mult).then_inc(use.drained, 1)

            def a_max(c, w):
                dve.wait_ge(scored.sem, scored.at(c, w + 1))
                dve.tensor_reduce(neg_max[:, w % 2, :], psum[4 + w % 2][:, :].rearrange("p (h j) -> p h j", h=HEADS),
                                  X_AXIS, ALU.max, negate=True).then_inc(max_ready.sem, 1)

            def a_divide(c, w):
                use = A[f"S{w}"]
                dve.wait_ge(use.filled, use.full(c))
                pv = use.bank[:, 0:72].rearrange("p (h c) -> p h c", h=HEADS)
                dve.reciprocal(rec[:, w % 2, :].unsqueeze(2), pv[:, :, 8:9]).then_inc(rec_ready.sem, 1)
                dve.wait_ge(rec_ready.sem, rec_ready.at(c, w + 1))
                dve.tensor_tensor(att[:, w, :].rearrange("p (h c) -> p h c", h=HEADS), pv[:, :, 0:8],
                                  rec[:, w % 2, :].unsqueeze(2).to_broadcast([128, HEADS, HD]),
                                  ALU.mult).then_inc(use.drained, 1)

            def a_attention(c):
                a_max(c, 0)
                a_max(c, 1)
                for w in range(NW):
                    a_divide(c, w)
                    if w + 2 < NW:
                        a_max(c, w + 2)

            def a_norm(c):
                st, done = st_a, ln1_dve
                use = A["proj"]
                dve.wait_ge(use.filled, use.full(c))
                dve.tensor_tensor(hid[:, :, :], use.bank[:, :].rearrange("p (w h) -> p w h", w=NW),
                                  h_bias[:, :].unsqueeze(1).to_broadcast([128, NW, C]), ALU.add)\
                   .then_inc(use.drained, 1)
                dve.wait_ge(A["proj"].drained, A["proj"].empty(c))
                dve.tensor_reduce(st[:, 0, :], hid[:, :, :], X_AXIS, ALU.add).then_inc(done.sem, 1)
                dve.wait_ge(done.sem, done.at(c, 1))
                dve.tensor_scalar(st[:, 1, :], st[:, 0, :], 1.0 / C, None, ALU.mult).then_inc(done.sem, 1)
                dve.wait_ge(ln1_act.sem, ln1_act.at(c, 1))
                dve.tensor_reduce(st[:, 2, :], sq[:, :, :], X_AXIS, ALU.add).then_inc(done.sem, 1)
                dve.wait_ge(done.sem, done.at(c, 3))
                dve.tensor_scalar(st[:, 10, :], st[:, 2, :], 1.0 / C, None, ALU.mult).then_inc(done.sem, 1)
                dve.tensor_scalar(st[:, 3, :], st[:, 2, :], 1.0 / C, LN_EPS, ALU.mult, ALU.add).then_inc(done.sem, 1)
                dve.wait_ge(ln1_act.sem, ln1_act.at(c, 3))
                refine(c, st, done, 5, 3, 5, 6, 7)
                dve.wait_ge(done.sem, done.at(c, 9))
                dve.tensor_tensor(st[:, 9, :], st[:, 10, :], st[:, 6, :], ALU.mult).then_inc(done.sem, 1)
                dve.wait_ge(done.sem, done.at(c, 10))
                dve.tensor_tensor(st[:, 14, :], st[:, 9, :], st[:, 6, :], ALU.mult).then_inc(done.sem, 1)
                dve.wait_ge(done.sem, done.at(c, 11))
                dve.tensor_scalar(st[:, 11, :], st[:, 14, :], 1.0, RMS_EPS, ALU.mult, ALU.add).then_inc(done.sem, 1)
                dve.wait_ge(ln1_act.sem, ln1_act.at(c, 5))
                refine(c, st, done, 12, 11, 13, 15, 16)
                dve.wait_ge(A["z1"].filled, A["z1"].full(c - 1))
                dve.tensor_scalar(xnT[:, 0:3], xnT[:, CH:CH + 3], col("keep")[:, bass.ds(c, 1)], None, ALU.mult)\
                   .then_inc(tail_kept.sem, 1)

            def a_softplus(c, h):
                dve.wait_ge(soft_act.sem, soft_act.at(c, 2 * h + 1))
                dve.tensor_scalar(w_d, ex_d, 1.0, None, ALU.add).then_inc(soft_dve.sem, 1)
                dve.wait_ge(soft_dve.sem, soft_dve.at(c, 2 * h + 1))
                dve.scalar_tensor_tensor(out=w_d, in0=w_d, scalar=-1.0, in1=ex_d,
                                         op0=ALU.add, op1=ALU.subtract).then_inc(soft_dve.sem, 1)

            def a_split(c, h):
                lo, hi = slice(0, 64), slice(64, 128)
                if h == 0:
                    dve.wait_ge(soft_pool.sem, soft_pool.at(c, 4))
                    src, dst = delta, delta_s
                else:
                    dve.wait_ge(xd_ready.sem, xd_ready.at(c, 1))
                    src, dst = xdel, xdel_s
                dve.tensor_copy(dst[lo, 0, :], src[lo, :]).then_inc(split_a.sem, 1)
                dve.tensor_copy(dst[hi, 1, :], src[hi, :]).then_inc(split_a.sem, 1)
                dve.wait_ge(split_a.sem, split_a.at(c, 2 * h + 2))
                dve.tensor_tensor(dst[hi, 0, :], src[lo, :], dst[lo, 0, :].bitcast(F32), ALU.subtract)\
                   .then_inc(split_b.sem, 1)
                dve.tensor_tensor(dst[lo, 1, :], src[hi, :], dst[hi, 1, :].bitcast(F32), ALU.subtract)\
                   .then_inc(split_b.sem, 1)

            def m_unit(c, n):
                h, (g, _, _) = n // NU, unit(n % NU)
                dve.wait_ge(xd_rep.sem, xd_rep.at(c, n + 1))
                if n == 0:
                    dve.wait_ge(A["b1"].drained, A["b1"].empty(c))
                    dve.wait_ge(stated.sem, stated.at(c, 1))
                dve.tensor_tensor(inject[:, n % 2, :], xd_ps[n % 2][:, :], b_rep[:, BAND * h:BAND * h + BAND], ALU.mult)\
                   .then_inc(injected.sem, 1)
                dve.wait_ge(injected.sem, injected.at(c, n + 1))
                dve.wait_ge(decayed.sem, decayed.at(c, n + 1))
                dve.wait_ge(stated.sem, stated.at(c, 1 + max(0, n - NU + 1)))
                dve.wait_ge(weighted.sem, weighted.at(c, n - 3))
                dve.wait_ge(stated.sem, stated.at(c, max(1, n - 2)))
                dve.tensor_tensor_scan(hs[:, n % 4, :], decay[:, n % 2, :], inject[:, n % 2, :],
                                       state[:, g:g + 1], ALU.mult, ALU.add).then_inc(scanned.sem, 1)

            def m_skip(c, h):
                dve.wait_ge(y_quads.sem, y_quads.at(c, 4 * h + 4))
                dve.wait_ge(gated.sem, gated.at(c, h))
                dve.scalar_tensor_tensor(out=y_skip[:, :], in0=xb[:, BAND * h:BAND * h + BAND], scalar=col("d_skip"),
                                         in1=y_ps[:, :], op0=ALU.mult, op1=ALU.add).then_inc(skipped.sem, 1)

            def f_front(c):
                st, done = st_f, ln2_dve
                use = F["mo"]
                dve.wait_ge(use.filled, use.full(c))
                dve.wait_ge(ln1_pool.sem, ln1_pool.at(c, 4))
                dve.tensor_tensor(h1[:, :, :], use.bank[:, :].rearrange("p (w h) -> p w h", w=NW), h_ln[:, :, :], ALU.add)\
                   .then_inc(use.drained, 1)

            def f_mean(c):
                st, done = st_f, ln2_dve
                dve.wait_ge(F["mo"].drained, F["mo"].empty(c))
                dve.tensor_reduce(st[:, 0, :], h1[:, :, :], X_AXIS, ALU.add).then_inc(done.sem, 1)
                dve.wait_ge(done.sem, done.at(c, 1))
                dve.tensor_scalar(st[:, 1, :], st[:, 0, :], 1.0 / C, None, ALU.mult).then_inc(done.sem, 1)

            def f_variance(c):
                st, done = st_f, ln2_dve
                dve.wait_ge(ln2_act.sem, ln2_act.at(c, 1))
                dve.tensor_reduce(st[:, 2, :], fsq[:, :, :], X_AXIS, ALU.add).then_inc(done.sem, 1)
                dve.wait_ge(done.sem, done.at(c, 3))
                dve.tensor_scalar(st[:, 3, :], st[:, 2, :], 1.0 / C, LN_EPS, ALU.mult, ALU.add).then_inc(done.sem, 1)

            def f_root(c):
                dve.wait_ge(ln2_act.sem, ln2_act.at(c, 3))
                refine(c, st_f, ln2_dve, 4, 3, 5, 6, 7)

            def f_route(c):
                st, done = st_f, route_dve
                wide = [128, NW, E]

                def wide_of(slot):
                    return st[:, slot, :].unsqueeze(2).to_broadcast(wide)

                count = [0]

                def link(ins):
                    ins.then_inc(done.sem, 1)
                    count[0] += 1
                    dve.wait_ge(done.sem, done.at(c, count[0]))

                use = F["lg"]
                dve.wait_ge(use.filled, use.full(c))
                rb2 = col("rb2").unsqueeze(1).to_broadcast(wide)
                rev = col("rev").unsqueeze(1).to_broadcast(wide)
                dve.tensor_tensor(rt[:, 0, :, :], use.bank[:, 0:NW * E].rearrange("p (w e) -> p w e", w=NW), rb2, ALU.add)\
                   .then_inc(use.drained, 1)
                dve.wait_ge(F["lg"].drained, F["lg"].empty(c))
                link(dve.tensor_reduce(st[:, 10, :], rt[:, 0, :, :], X_AXIS, ALU.max))
                link(dve.tensor_tensor(rt[:, 1, :, :], rt[:, 0, :, :], wide_of(10), ALU.subtract))
                link(dve.memset(rt[:, 12, :, :], 0.0))
                dve.wait_ge(route_act.sem, route_act.at(c, 1))
                link(dve.tensor_reduce(st[:, 11, :], rt[:, 2, :, :], X_AXIS, ALU.add))
                link(dve.reciprocal(st[:, 12, :], st[:, 11, :]))
                link(dve.tensor_tensor(rt[:, 3, :, :], rt[:, 2, :, :], wide_of(12), ALU.mult))
                link(dve.tensor_reduce(st[:, 16, :], rt[:, 3, :, :], X_AXIS, ALU.max))
                link(dve.tensor_tensor(rt[:, 4, :, :], rt[:, 3, :, :], wide_of(16), ALU.is_equal))
                link(dve.tensor_tensor(rt[:, 5, :, :], rt[:, 4, :, :], rev, ALU.mult))
                link(dve.tensor_reduce(st[:, 10, :], rt[:, 5, :, :], X_AXIS, ALU.max))
                link(dve.tensor_tensor(rt[:, 6, :, :], rt[:, 5, :, :], wide_of(10), ALU.is_equal))
                link(dve.scalar_tensor_tensor(out=rt[:, 7, :, :], in0=rt[:, 6, :, :], scalar=-2.0, in1=rt[:, 3, :, :],
                                              op0=ALU.mult, op1=ALU.add))
                link(dve.tensor_reduce(st[:, 17, :], rt[:, 7, :, :], X_AXIS, ALU.max))
                link(dve.tensor_tensor(st[:, 13, :], st[:, 17, :], st[:, 16, :], ALU.subtract))
                link(dve.tensor_tensor(rt[:, 8, :, :], rt[:, 7, :, :], wide_of(17), ALU.is_equal))
                link(dve.tensor_tensor(rt[:, 9, :, :], rt[:, 8, :, :], rev, ALU.mult))
                link(dve.tensor_reduce(st[:, 10, :], rt[:, 9, :, :], X_AXIS, ALU.max))
                link(dve.tensor_tensor(rt[:, 10, :, :], rt[:, 9, :, :], wide_of(10), ALU.is_equal))
                dve.wait_ge(route_act.sem, route_act.at(c, 2))
                link(dve.tensor_scalar(st[:, 15, :], st[:, 14, :], 1.0, None, ALU.add))
                link(dve.reciprocal(st[:, 18, :], st[:, 15, :]))
                link(dve.tensor_tensor(rt[:, 11, :, :], rt[:, 10, :, :], wide_of(14), ALU.mult))
                link(dve.tensor_tensor(rt[:, 12, :, :], rt[:, 11, :, :], rt[:, 6, :, :], ALU.add))
                link(dve.tensor_tensor(rt[:, 13, :, :], rt[:, 12, :, :], wide_of(18), ALU.mult))
                link(dve.tensor_copy(w_parts[:, :, 0, :], rt[:, 13, :, :]))
                link(dve.tensor_tensor(w_parts[:, :, 1, :], rt[:, 13, :, :], w_parts[:, :, 0, :].bitcast(F32),
                                       ALU.subtract))

            def f_expert(c, s, e):
                use = F[f"wb_{s}{e}"]
                dve.wait_ge(use.filled, use.full(c))
                dve.wait_ge(F[f"h2_{s}{e}"].drained, F[f"h2_{s}{e}"].empty(c))
                dve.tensor_tensor(ew[:, s, e, :], e2[:, (EP * s + e) % 2, :], use.bank[:, :], ALU.mult)\
                   .then_inc(use.drained, 1)

            def f_out(c):
                use = F["out"]
                dve.wait_ge(use.filled, use.full(c))
                dve.wait_ge(stored.sem, stored.at(c - 1, 256))
                dve.tensor_tensor(res[:, :, :], use.bank[:, :].rearrange("p (w h) -> p w h", w=NW), h1[:, :, :],
                                  ALU.add).then_inc(use.drained, 1)

            def f_step(c, n):
                if n == F_AT["mean"]:
                    f_mean(c)
                if n == F_AT["variance"]:
                    f_variance(c)
                if n == F_AT["root"]:
                    f_root(c)
                if n == F_AT["route"]:
                    f_route(c)
                if n in F_EXPERT:
                    f_expert(c, *F_EXPERT[n])
                if n == F_AT["out"]:
                    f_out(c)

            def chunk(c, experts):
                a_rope(c)
                a_attention(c)
                a_norm(c)
                a_softplus(c, 0)
                a_softplus(c, 1)
                a_split(c, 0)
                a_split(c, 1)
                for n in range(2 * NU):
                    m_unit(c, n)
                    if n == NU + 3:
                        m_skip(c, 0)
                    if experts:
                        f_step(c - 1, n)
                m_skip(c, 1)
                f_front(c)

            dve.wait_ge(loaded, 16)
            dve.wait_ge(staged, 16)
            dve.tensor_copy(ident_r[:, :], col("ident")).then_inc(setup_dve, 1)
            dve.tensor_copy(unit_sel[:, :, :], staging[:, 0:1024].rearrange("p (a b) -> p a b", a=8)).then_inc(setup_dve, 1)
            dve.tensor_copy(w_sel[:, :, :], staging[0:2 * E, 1024:1024 + EP * 128].rearrange("p (a b) -> p a b", a=EP))\
               .then_inc(setup_dve, 1)
            dve.tensor_scalar(conv_w[:, 0, :], col("conv_in"), col("normw"), None, ALU.mult).then_inc(setup_dve, 1)
            dve.tensor_scalar(z_w[:, :], col("z_in"), col("normw"), None, ALU.mult).then_inc(setup_dve, 1)
            dve.wait_ge(setup_dve, 4)
            dve.tensor_tensor(conv_w[:, 1, :], conv_w[:, 0, :], col("conv_tap", 128, 256), ALU.mult)\
               .then_inc(setup_dve, 1)
            dve.wait_ge(setup_dve, 6)
            dve.tensor_tensor(conv_w[:, 0, :], conv_w[:, 0, :], col("conv_tap", 0, 128), ALU.mult)\
               .then_inc(setup_dve, 1)
            dve.wait_ge(setup_pe, 1)
            dve.tensor_copy(h_bias[:, :], y_ps[:, 0:C]).then_inc(setup_dve, 1)
            dve.memset(xnT[:, :], 0.0).then_inc(setup_dve, 1)
            dve.wait_ge(setup_dve, 9)
            dve.wait_ge(setup_pool, 4)
            chunk(0, False)
            with dve.Fori(1, NCH) as c:
                chunk(c, True)
            for n in range(2 * NU):
                f_step(NCH - 1, n)

        @block.gpsimd
        def _(pool):
            def a_rope(c):
                pool.wait_ge(A["q2"].drained, A["q2"].empty(c))
                pool.wait_ge(A["q"].drained, A["q"].empty(c))
                pool.wait_ge(scored.sem, scored.at(c - 1, NW))
                for half in range(2):
                    p = slice(64 * half, 64 * half + 64)
                    pool.wait_ge(q_ready.sem, q_ready.at(c, half))
                    pool.tensor_tensor(q_diag[p, :, 64 * half:64 * half + 64],
                                       rot[p, 0, :].rearrange("p (w i) -> p w i", w=NW),
                                       rot[p, 1, :].rearrange("p (w i) -> p w i", w=NW), ALU.add)\
                        .then_inc(q_ready.sem, 1)
                pool.wait_ge(q_ready.sem, q_ready.at(c, 2))
                pool.wait_ge(A["k2"].drained, A["k2"].empty(c))
                pool.wait_ge(A["k"].drained, A["k"].empty(c))
                pool.wait_ge(k_ready.sem, k_ready.at(c - 1, 1 + HEADS))
                pool.tensor_tensor(k_rot[:, :], rot[:, 2, :], rot[:, 3, :], ALU.add).then_inc(k_ready.sem, 1)

            def center(c, src, mean, dst, done):
                pool.tensor_tensor(dst[:, :, :], src[:, :, :], mean.unsqueeze(2).to_broadcast([128, NW, C]),
                                   ALU.subtract).then_inc(done.sem, 1)

            def scale(c, src, r, dst, done):
                pool.tensor_tensor(dst[:, :, :], src[:, :, :], r.unsqueeze(2).to_broadcast([128, NW, C]),
                                   ALU.mult).then_inc(done.sem, 1)

            def a_norm(c):
                pool.wait_ge(ln1_dve.sem, ln1_dve.at(c, 2))
                center(c, hid, st_a[:, 1, :], cen, ln1_pool)
                pool.wait_ge(ln1_dve.sem, ln1_dve.at(c, 9))
                pool.wait_ge(ln1_pool.sem, ln1_pool.at(c, 1))
                scale(c, cen, st_a[:, 6, :], lnx, ln1_pool)
                pool.wait_ge(ln1_dve.sem, ln1_dve.at(c, 16))
                pool.wait_ge(ln1_pool.sem, ln1_pool.at(c, 2))
                scale(c, lnx, st_a[:, 15, :], xn, ln1_pool)
                pool.tensor_tensor(h_ln[:, :, :], hid[:, :, :], lnx[:, :, :], ALU.add).then_inc(ln1_pool.sem, 1)

            def a_softplus(c, h):
                at = slice(BAND * h, BAND * h + BAND)
                pool.wait_ge(soft_act.sem, soft_act.at(c, 2 * h + 2))
                pool.wait_ge(soft_dve.sem, soft_dve.at(c, 2 * h + 2))
                pool.tensor_tensor(ln_d, ln_d, w_d, ALU.subtract).then_inc(soft_pool.sem, 1)
                pool.wait_ge(soft_pool.sem, soft_pool.at(c, 2 * h + 1))
                pool.tensor_tensor(delta[:, at], ln_d, relu_d, ALU.add).then_inc(soft_pool.sem, 1)

            def a_xdelta(c):
                pool.wait_ge(soft_pool.sem, soft_pool.at(c, 4))
                pool.tensor_tensor(xdel[:, :], delta[:, :], xb[:, :], ALU.mult).then_inc(xd_ready.sem, 1)

            def m_start(c):
                pool.tensor_tensor(state[:, :], state[:, :], col("keep")[:, bass.ds(c, 1)].to_broadcast([128, NU]),
                                   ALU.mult)\
                    .then_inc(stated.sem, 1)

            def m_unit(c, n):
                h, (g, _, _) = n // NU, unit(n % NU)
                pool.wait_ge(scanned.sem, scanned.at(c, n + 1))
                if n == 0:
                    pool.wait_ge(A["c1"].drained, A["c1"].empty(c))
                pool.wait_ge(y_quads.sem, y_quads.at(c, n // 4 - 1))
                pool.tensor_tensor(hc[:, n % 8, :], hs[:, n % 4, :], c_rep[:, BAND * h:BAND * h + BAND], ALU.mult)\
                    .then_inc(weighted.sem, 1)
                pool.tensor_copy(state[:, g:g + 1], hs[:, n % 4, BAND - 1:BAND]).then_inc(stated.sem, 1)

            def m_gate(c, h):
                pool.wait_ge(skipped.sem, skipped.at(c, h + 1))
                order = "p (i w j) -> p w i j"
                pool.tensor_tensor(y_gated[:, :, h, :].rearrange("p w (i j) -> p w i j", i=8),
                                   y_skip[:, :].rearrange(order, i=8, w=8),
                                   gate[:, BAND * h:BAND * h + BAND].rearrange(order, i=8, w=8), ALU.mult)\
                    .then_inc(gated.sem, 1)

            def f_center(c):
                pool.wait_ge(ln2_dve.sem, ln2_dve.at(c, 2))
                center(c, h1, st_f[:, 1, :], fcen, ln2_pool)

            def f_scale(c):
                pool.wait_ge(ln2_dve.sem, ln2_dve.at(c, 8))
                pool.wait_ge(ln2_pool.sem, ln2_pool.at(c, 1))
                scale(c, fcen, st_f[:, 6, :], fn, ln2_pool)

            def f_step(c, n):
                if n == F_AT["mean"]:
                    f_center(c)
                if n == F_AT["root"]:
                    f_scale(c)

            def chunk(c, experts):
                a_rope(c)
                a_norm(c)
                a_softplus(c, 0)
                a_softplus(c, 1)
                a_xdelta(c)
                m_start(c)
                for n in range(2 * NU):
                    m_unit(c, n)
                    if n == NU + 3:
                        m_gate(c, 0)
                    if experts:
                        f_step(c - 1, n)
                m_gate(c, 1)

            pool.memset(q_diag[:, :, :], 0.0).then_inc(setup_pool, 1)
            pool.memset(v_diag[:, :, :, :], 0.0).then_inc(setup_pool, 1)
            for half in range(2):
                pool.wait_ge(setup_pool, 2 + half)
                pool.memset(v_diag[64 * half:64 * half + 64, :, :, 9 * half + 8:9 * half + 9], 1.0)\
                    .then_inc(setup_pool, 1)
            pool.wait_ge(setup_pool, 4)
            pool.memset(state[:, :], 0.0).then_inc(setup_pool, 1)
            pool.wait_ge(setup_pool, 5)
            pool.wait_ge(setup_dve, 9)
            chunk(0, False)
            with pool.Fori(1, NCH) as c:
                chunk(c, True)
            for n in range(2 * NU):
                f_step(NCH - 1, n)


def pack(v):
    w = np.zeros((128, N_PACKED), np.float32)
    s = np.zeros((128, N_SELECT), np.float32)

    def put(name, a, row=0, at=0):
        lo = COL[name][0] + at
        w[row:row + a.shape[0], lo:lo + a.shape[1]] = a

    eye = np.eye(128, dtype=np.float32)
    put("ident", eye)
    swap = [i + 1 - 2 * (i % 2) for i in range(C)]
    qkv, qb = v["L0_tok_qkv_w"], v["L0_tok_qkv_b"]
    parts = [qkv[0:C], qkv[0:C][swap], qkv[C:2 * C], qkv[C:2 * C][swap]]
    biases = [qb[0:C], qb[0:C][swap], qb[C:2 * C], qb[C:2 * C][swap]]
    for half in range(2):
        at = 64 * half
        for n, name in enumerate(("wq", "wq2", "wk", "wk2")):
            put(name, parts[n].T, at, at)
            put("bias_qk", biases[n][:, None], at, n)
        for h in range(HEADS):
            wv = qkv[2 * C + HD * h:2 * C + HD * h + HD].T
            put("wv", wv, at, 64 * (h % 2) + 32 * half + 8 * (h // 2))
        put("wp", v["L0_tok_proj_w"].T, at, at)
    pos = np.arange(WIN, dtype=np.float32)
    freq = (1.0 / 10000.0 ** (np.arange(0, HD // 2, 2, dtype=np.float32) / (HD // 2))).astype(np.float32)
    for ch in range(128):
        c = ch % HD
        ang = pos * freq[(c % 4) // 2]
        ang = np.repeat(ang, WIN) if c < 4 else np.tile(ang, WIN)
        w[ch, COL["cos"][0]:COL["cos"][1]] = np.cos(ang)
        w[ch, COL["sin"][0]:COL["sin"][1]] = np.sin(ang) if c % 2 else -np.sin(ang)
        w[ch, COL["headmask"][0] + (ch % 64) // HD] = 1.0
    put("bv_rep", np.broadcast_to(qb[2 * C:][:, None], (C, 128)))
    put("bv_rep", np.ones((1, 128), np.float32), C)
    put("wp_row", v["L0_tok_proj_w"].T)
    put("wp_row", v["L0_tok_proj_b"][None], C)
    inw, cw = v["L0_attn_in_proj_w"], v["L0_attn_conv_w"]
    for half in range(2):
        put("normw", v["L0_attn_norm_w"][:, None], 64 * half)
        put("conv_in", inw[0:DI].T, 64 * half)
        for pair in range(2):
            tap = TAPS - 1 - 2 * pair - half
            put("conv_tap", np.broadcast_to(cw[:, 0, tap][None], (64, DI)), 64 * half, 128 * pair)
    put("z_in", inw[DI:].T)
    put("conv_b", v["L0_attn_conv_b"][:, None])
    put("delta_b", v["L0_attn_projDelta_b"][:, None])
    put("d_skip", v["L0_attn_D"][:, None])
    put("wdelta", v["L0_attn_projDelta_w"].T)
    put("wb", np.repeat(v["L0_attn_projB_w"].T, GD, axis=1))
    put("wc", np.repeat(v["L0_attn_projC_w"].T, GD, axis=1))
    put("a_log", v["L0_attn_A_log"].reshape(NU, GD, NS).transpose(2, 1, 0).reshape(128, NU))
    for n in range(NS):
        for d in range(GD):
            for i in range(4):
                w[GD * n + d, COL["y_sel"][0] + 32 * i + 8 * i + d] = 1.0
            for g in range(8):
                for half in range(2):
                    s[64 * half + 8 * g + d, 128 * g + GD * n + d] = 1.0
    put("w_out", v["L0_attn_out_proj_w"].T)
    for k in range(2):
        put("rw1", v["L0_ffn_router_w1"], 64 * k, RH * k)
    put("rb1", v["L0_ffn_router_b1"][:, None])
    put("rw2", v["L0_ffn_router_w2"])
    put("rb2", np.broadcast_to(v["L0_ffn_router_b2"][None], (128, E)))
    put("rev", np.broadcast_to(np.arange(E, 0, -1, dtype=np.float32)[None], (128, E)))
    for e in range(E):
        p, o = e // 2, 64 * (e % 2)
        for k in range(2):
            put("ew1", v["L0_ffn_expert_w1"][e], 64 * k, 128 * (EP * k + p) + o)
        put("ew2", v["L0_ffn_expert_w2"][e], o, 128 * p + o)
        put("ew3", v["L0_ffn_expert_w3"][e], o, C * p)
        put("eb1", v["L0_ffn_expert_b1"][e][:, None], o, p)
        put("eb2", v["L0_ffn_expert_b2"][e][:, None], o, p)
        for t in range(NW):
            put("eb3", v["L0_ffn_expert_b3"][e][None], E * t + e, C * t)
        for part in range(2):
            at = SEL["w_sel"][0] + 128 * p + o
            s[E * part + e, at:at + 64] = 1.0
    for c in range(NCH):
        if c % PER_IMAGE:
            w[:, COL["keep"][0] + c] = 1.0
    return w, s


def kernel(**inputs):
    import concourse.bacc as bacc
    from concourse.bass_utils import run_bass_kernel_spmd

    v = {name: np.ascontiguousarray(a) for name, a in inputs.items()}
    packed, select = pack(v)
    arrays = {"x": v["x"].reshape(B * IMG, IMG, C), "packed": packed, "select": select}
    nc = bacc.Bacc("TRN2", target_bir_lowering=False, num_devices=1)
    args = [nc.dram_tensor(f"in_{n}_dram", a.shape, F32, kind="ExternalInput").ap() for n, a in arrays.items()]
    out = nc.dram_tensor("out_dram", (B * IMG, IMG, C), F32, kind="ExternalOutput").ap()
    tower(nc, *args, out)
    r = run_bass_kernel_spmd(nc, [{f"in_{n}_dram": a for n, a in arrays.items()}], core_ids=[0])
    return r.results[0]["out_dram"].reshape(B, L, C)
```
